# Optimizing a Trainium2 kernel written in Bass

```python
import numpy as np
import jax
import jax.numpy as jnp

def _softmax(x, axis=-1):
    return jax.nn.softmax(x, axis=axis)

def _gelu(x):
    return jax.nn.gelu(x, approximate=True)

def _silu(x):
    return jax.nn.silu(x)

def _sigmoid(x):
    return jax.nn.sigmoid(x)

def _layernorm(x, axis=-1, eps=1e-05):
    m = jnp.mean(x, axis=axis, keepdims=True)
    v = jnp.var(x, axis=axis, keepdims=True)
    return (x - m) / jnp.sqrt(v + eps)

def _scatter_add(tgt, idx, src, axis=0):
    return tgt.at[idx].add(src)

def _segment_sum(src, seg, n):
    return jax.ops.segment_sum(src, seg, n)
kernel_name = 'mk_adj_preln_d4_adj_r2_d5c449'

def setup_inputs(seed: int=0):
    np.random.seed(seed)
    _w = jnp.asarray

    def _rec_inputs():
        import jax
        import jax.numpy as jnp
        _gk = jax.random.key(seed)
        x = -0.000929 + 1 * jax.random.normal(jax.random.fold_in(_gk, 1), (8192, 64), jnp.float32)
        _a = jax.random.bernoulli(jax.random.fold_in(_gk, 2), 0.000244141, (8192, 8192))
        _a = jnp.logical_or(_a, jnp.eye(8192, dtype=bool))
        _af = _a.astype(jnp.float32)
        _af = _af * jax.random.uniform(jax.random.fold_in(_gk, 3), (8192, 8192), jnp.float32, 0.05, 1)
        adj = _af
        return (x, adj)
    x, adj = _rec_inputs()

    def _L0_gnn_setup():
        import jax, jax.numpy as jnp
        import numpy as np
        P_DROP = 0.1
        key = jax.random.key(seed)
        k1, k2, k3 = jax.random.split(key, 3)
        N, D = (8192, 64)
        x = jax.random.normal(k1, (N, D), dtype=jnp.float32)
        adj = jax.random.uniform(k2, (N, N), dtype=jnp.float32)
        u = jax.random.uniform(k3, (N, D), dtype=jnp.float32)
        return {'x': x, 'adj': adj, 'u': u}
    _L0_gnn_all = _L0_gnn_setup()
    _L0_gnn_in = {k: v for k, v in _L0_gnn_all.items() if k in ('u',)}
    del _L0_gnn_all

    def _L1_gnn_setup():
        import jax, jax.numpy as jnp
        import numpy as np
        N = 8192
        D_IN = 64
        D_OUT = 64
        EDGE_P = 0.002
        key = jax.random.key(seed)
        kx, ka, kw = jax.random.split(key, 3)
        X = jax.random.normal(kx, (N, D_IN), dtype=jnp.float32)
        adj = (jax.random.uniform(ka, (N, N)) < EDGE_P).astype(jnp.float32)
        W = jax.random.normal(kw, (D_OUT, 2 * D_IN), dtype=jnp.float32) * (1.0 / np.sqrt(2 * D_IN))
        return {'X': X, 'adj': adj, 'W': W}
    _L1_gnn_all = _L1_gnn_setup()
    _L1_gnn_in = {k: v for k, v in _L1_gnn_all.items() if k in ('W',)}
    del _L1_gnn_all

    def _L2_gnn_setup():
        import jax, jax.numpy as jnp
        import numpy as np
        N = 5000
        DIM = 64
        F_CONST = 1.0
        B_CONST = 0.1
        R_CONST = 0.01
        key = jax.random.key(seed)
        k1, k2 = jax.random.split(key)
        t = jnp.zeros((1,), dtype=jnp.float32)
        x = jax.random.uniform(k1, (N, DIM), dtype=jnp.float32)
        A = jax.random.uniform(k2, (N, N), dtype=jnp.float32)
        return {'t': t, 'x': x, 'A': A}
    _L2_gnn_all = _L2_gnn_setup()
    _L2_gnn_in = {k: v for k, v in _L2_gnn_all.items() if k in ('t',)}
    del _L2_gnn_all

    def _L3_gnn_setup():
        import jax, jax.numpy as jnp
        import numpy as np
        N = 4096
        DIN = 64
        DH = 64
        DOUT = 64
        SPARSITY = 0.01
        key = jax.random.key(seed)
        ks = jax.random.split(key, 9)
        x = jax.random.normal(ks[0], (N, DIN), dtype=jnp.float32)
        A = (jax.random.uniform(ks[1], (N, N)) < SPARSITY).astype(jnp.float32)
        left_weights = jax.random.normal(ks[2], (N, N), dtype=jnp.float32)

        def lin(k, fan_in, fan_out):
            k1, k2 = jax.random.split(k)
            bound = 1.0 / np.sqrt(fan_in)
            W = jax.random.uniform(k1, (fan_out, fan_in), minval=-bound, maxval=bound, dtype=jnp.float32)
            b = jax.random.uniform(k2, (fan_out,), minval=-bound, maxval=bound, dtype=jnp.float32)
            return (W, b)
        W0, b0 = lin(ks[3], DIN, DH)
        W1, b1 = lin(ks[4], DH, DH)
        W2, b2 = lin(ks[5], DH, DOUT)
        return {'x': x, 'A': A, 'left_weights': left_weights, 'W0': W0, 'b0': b0, 'W1': W1, 'b1': b1, 'W2': W2, 'b2': b2}
    _L3_gnn_all = _L3_gnn_setup()
    _L3_gnn_in = {k: v for k, v in _L3_gnn_all.items() if k in ('W0', 'b0', 'W1', 'b1', 'W2', 'b2')}
    del _L3_gnn_all
    return {'x': x, 'adj': adj, 'L0_gnn_u': _L0_gnn_in['u'], 'L1_gnn_W': _L1_gnn_in['W'], 'L2_gnn_t': _L2_gnn_in['t'], 'L3_gnn_W0': _L3_gnn_in['W0'], 'L3_gnn_b0': _L3_gnn_in['b0'], 'L3_gnn_W1': _L3_gnn_in['W1'], 'L3_gnn_b1': _L3_gnn_in['b1'], 'L3_gnn_W2': _L3_gnn_in['W2'], 'L3_gnn_b2': _L3_gnn_in['b2']}

def reference(x, adj, L0_gnn_u, L1_gnn_W, L2_gnn_t, L3_gnn_W0, L3_gnn_b0, L3_gnn_W1, L3_gnn_b1, L3_gnn_W2, L3_gnn_b2):
    import jax
    import jax.numpy as jnp

    def _L0_gnn_ref(x, adj, u):
        import jax, jax.numpy as jnp
        import numpy as np
        P_DROP = 0.1
        keep = (u >= P_DROP).astype(x.dtype)
        x_drop = x * keep / (1.0 - P_DROP)
        return jnp.matmul(adj, x_drop)

    def _L1_gnn_ref(X, adj, W):
        import jax, jax.numpy as jnp
        import numpy as np
        N = 8192
        D_IN = 64
        D_OUT = 64
        EDGE_P = 0.002
        deg = jnp.sum(adj, axis=1, keepdims=True)
        nb_agg = adj @ X / jnp.maximum(deg, 1.0)
        X_cat = jnp.concatenate([X, nb_agg], axis=1)
        out = X_cat @ W.T
        return jax.nn.relu(out)

    def _L2_gnn_ref(t, x, A):
        import jax, jax.numpy as jnp
        import numpy as np
        N = 5000
        DIM = 64
        F_CONST = 1.0
        B_CONST = 0.1
        R_CONST = 0.01
        Ax = A @ x
        outer = R_CONST * jnp.sum(x * Ax, axis=1, keepdims=True)
        return F_CONST - B_CONST * x - outer

    def _L3_gnn_ref(x, A, left_weights, W0, b0, W1, b1, W2, b2):
        import jax, jax.numpy as jnp
        import numpy as np
        N = 4096
        DIN = 64
        DH = 64
        DOUT = 64
        SPARSITY = 0.01
        w = left_weights * A
        for W, b in ((W0, b0), (W1, b1), (W2, b2)):
            x = w @ x
            x = x @ W.T + b
        return x
    h = jnp.maximum(_layernorm(x, axis=-1), 0.0)
    x = x + _L0_gnn_ref(h, adj, L0_gnn_u)
    h = jnp.maximum(_layernorm(x, axis=-1), 0.0)
    x = x + _L1_gnn_ref(h, adj, L1_gnn_W)
    h = jnp.maximum(_layernorm(x, axis=-1), 0.0)
    x = x + _L2_gnn_ref(L2_gnn_t, h, adj)
    h = jnp.maximum(_layernorm(x, axis=-1), 0.0)
    x = x + _L3_gnn_ref(h, adj, adj, L3_gnn_W0, L3_gnn_b0, L3_gnn_W1, L3_gnn_b1, L3_gnn_W2, L3_gnn_b2)
    return x

_drawn_inputs = setup_inputs


def setup_inputs(seed=0):
    import zlib

    import numpy as np

    out = dict(_drawn_inputs(seed))
    spreads = {}
    factors = {}
    for name, (base, spread) in spreads.items():
        noise = np.random.default_rng([zlib.crc32(name.encode()), seed]).standard_normal(out[name].shape)
        drawn = base * np.exp(spread * noise) if base else spread * noise
        out[name] = jnp.asarray(drawn.astype(out[name].dtype))
    for name, factor in factors.items():
        out[name] = (out[name] * factor).astype(out[name].dtype)
    return out
```

```python
from contextlib import ExitStack

import concourse.bass as bass
from concourse import mybir

P = 128
N = 8192
D = 64
TILES = N // P
BT = 8
BLOCK = BT * P
BLOCKS = N // BLOCK
PASSES = 6
DEG_PASS, RELU_PASS, OUTER_PASS = 1, 2, 3
SQUARED_FROM = 4
LINEAR = {2: 0, 4: 1, 5: 2, 6: 3}
HW = 2 * D + 2
KEEP_FROM = 0.1
KEEP_SCALE = 1.0 / 0.9
EPS = 1e-5

ALU = mybir.AluOpType
ACT = mybir.ActivationFunctionType
AX = mybir.AxisListType.X
F32 = mybir.dt.float32



def bodies_before(s, r):
    if s == 1:
        return BLOCKS * r
    return BLOCKS * BLOCKS + (s - 2) * (BLOCKS * (BLOCKS + 1) // 2) + r * (r + 1) // 2


def squares_before(s, r):
    if s == 3:
        return r * (r - 1) // 2
    return BLOCKS * (BLOCKS - 1) // 2 + (s - 4) * (BLOCKS * (BLOCKS + 1) // 2) + r * (r + 1) // 2


def in_register(eng, value, top):
    if static(value):
        return value
    return eng.snap(eng.to_reg(value), donate=True, min_val=0, max_val=top)


def place(eng, s, r):
    return r if s % 2 else in_register(eng, BLOCKS - 1 - r, BLOCKS - 1)


def row_blocks(eng, row):
    row(0, 0)
    with eng.Fori(0, BLOCKS // 2 - 1) as i:
        row(eng.snap(2 * i + 1), 1)
        row(eng.snap(2 * i + 2), 0)
    row(BLOCKS - 1, 1)


def static(r):
    return isinstance(r, int)


def build(nc, x_d, adj_d, u_d, w2_d, wl_d, eye_d, out_d):
    with ExitStack() as ctx:
        def sb(name, shape):
            return ctx.enter_context(nc.sbuf_tensor(name, shape, F32))

        def ps(name, shape):
            return ctx.enter_context(nc.psum_tensor(name, shape, F32))

        def sem(name):
            return ctx.enter_context(nc.semaphore(name))

        adj = sb("adj", [P, BT, BLOCK])
        sq = sb("sq", [P, BT, BLOCK])
        h = sb("h", [P, TILES, HW])
        x = sb("x", [P, TILES, D])
        partial = sb("partial", [P, TILES, D])
        rdeg = sb("rdeg", [P, TILES])
        cat = sb("cat", [P, BT, 2 * D])
        ycat = sb("ycat", [P, BT, 2 * D])
        lhs = sb("lhs", [P, BLOCK])
        w2 = sb("w2", [P, D])
        wl = sb("wl", [D + 1, 3, D])
        eye = sb("eye", [P, P])
        xc = sb("xc", [P, BT, D])
        xsq = sb("xsq", [P, BT, D])
        rsum = sb("rsum", [P, BT])
        mneg = sb("mneg", [P, BT])
        vsum = sb("vsum", [P, BT])
        var = sb("var", [P, BT])
        std = sb("std", [P, BT])
        r0 = sb("r0", [P, BT])
        nt = sb("nt", [P, BT])
        rstd = sb("rstd", [P, BT])
        epsc = sb("epsc", [P, 1])

        acc = ps("acc", [P, 4 * 512])
        turned = ps("turned", [P, BLOCK])
        lin = ps("lin", [P, BT * D])

        adj_loaded = [sem(f"adj_loaded{k}") for k in range(BT)]
        x_loaded = sem("x_loaded")
        u_loaded = sem("u_loaded")
        weights_loaded = sem("weights_loaded")
        adj_used = sem("adj_used")
        squared = sem("squared")
        sq_used = sem("sq_used")
        consts_set = sem("consts_set")
        acc_read = sem("acc_read")
        h_ready = sem("h_ready")
        y_ready = sem("y_ready")
        y_turned = sem("y_turned")
        lhs_ready = sem("lhs_ready")
        lin_done = sem("lin_done")
        var_ready = sem("var_ready")
        std_ready = sem("std_ready")
        step = sem("step")
        out_ready = sem("out_ready")
        stored = sem("stored")

        h_two = [h[:, :, c * D:(c + 1) * D] for c in range(2)]

        def acc_tiles(s, parity):
            if s == DEG_PASS:
                return acc[:, :].rearrange("p (t c) -> p t c", t=BT)
            return acc[:, parity * 1024:(parity + 1) * 1024].rearrange("p (t c) -> p t c", t=BT)

        block = ctx.enter_context(nc.Block())

        @block.sync
        def _(sp):
            def load(s, g, b, rb, jb):
                for k in range(BT):
                    tile = in_register(sp, rb * TILES + jb * BT + k, BLOCKS * TILES - 1)
                    squares = in_register(sp, BT * b + k + 1, 1 << 14)
                    if s <= 4:
                        sp.wait_ge(adj_used, BT * g + k + 1 if s <= 3 else BT * bodies_before(4, 0) + k + 1)
                    if s >= 3:
                        sp.wait_ge(squared, squares)
                    sp.dma_start(adj[:, k, :], adj_d[tile]).then_inc(adj_loaded[k], 16)

            for s in range(1, PASSES + 1):
                def row(r, parity, s=s):
                    g = bodies_before(s, r)
                    b = squares_before(s, r) if s >= 3 else 0
                    g = g if static(r) else sp.snap(g)
                    b = b if static(b) else sp.snap(b)
                    rb = place(sp, s, r)
                    load(s, g, b, rb, rb)
                    if s == 1 and not (static(r) and r == BLOCKS - 1):
                        with sp.Fori(r + 1, BLOCKS) as j:
                            load(s, (BLOCKS - 1) * r + j, 0, rb, j)
                    if not (static(r) and r == 0):
                        with sp.Fori(0, r) as j:
                            load(s, (BLOCKS - 1) * r + BLOCKS + j if s == 1 else g + 1 + j, b + j if s == 3 else b + 1 + j,
                                 rb, place(sp, s, j))
                row_blocks(sp, row)

        @block.tensor
        def _(pe):
            def body(s, g, b, jb, parity, corner, single):
                tiles = acc_tiles(s, parity)
                own, nxt = s % 2, (s + 1) % 2
                for k in range(BT):
                    jt = jb * BT + k
                    off = jt * HW
                    hflat = h[:, :, :].rearrange("p t c -> p (t c)")
                    raw = s <= 3
                    start = corner is not None and k == 0
                    if raw:
                        pe.wait_ge(adj_loaded[k], 16 * g + 16)
                        if single:
                            lo, n = own * D, D
                        elif s < 3:
                            lo, n = 0, 2 * D
                        else:
                            lo, n = own * D, D
                        if s == DEG_PASS:
                            n = n + 1
                        for t in range(BT):
                            last = nc.tensor.matmul(
                                tiles[:, t, lo:lo + n], adj[:, k, t * P:(t + 1) * P], hflat[:, bass.ds(off + lo, n)],
                                start=start and t % (2 if s == 1 else 4) == 0, stop=False, skip_group_check=True)
                        last.then_inc(adj_used, 1)
                    if s > 3 or (s == 3 and not single):
                        pe.wait_ge(squared, BT * b + BT + k + 1)
                        if s == 3:
                            lo, n = nxt * D, D
                        elif single:
                            lo, n = own * D, D
                        else:
                            lo, n = 0, 2 * D
                        for t in range(BT):
                            last = nc.tensor.matmul(
                                tiles[:, t, lo:lo + n], sq[:, k, t * P:(t + 1) * P], hflat[:, bass.ds(off + lo, n)],
                                start=start and t % 4 == 0, stop=False, skip_group_check=True)
                        last.then_inc(sq_used, 1)
                    if corner and k == BT // 2 - 1:
                        corner[0]()
                    if corner and k == BT - 1:
                        corner[1]()

            def turn(s, n):
                src = cat if s == RELU_PASS else ycat
                pe.wait_ge(y_ready, n + 1)
                for t in range(BT):
                    last = nc.tensor.transpose(turned[:, t * P:(t + 1) * P], src[:, t, :], eye[:, :])
                last.then_inc(y_turned, 1)

            def linear(s, n):
                k = P if s == RELU_PASS else D + 1
                w = w2[:, :] if s == RELU_PASS else wl[:, LINEAR[s] - 1, :]
                pe.wait_ge(lhs_ready, n + 1)
                for t in range(BT):
                    last = nc.tensor.matmul(lin[:, t * D:(t + 1) * D], lhs[0:k, t * P:(t + 1) * P], w[0:k, :],
                                            start=True, stop=True)
                last.then_inc(lin_done, 1)

            pe.wait_ge(consts_set, 1)
            pe.wait_ge(weights_loaded, 48)
            nothing = (lambda: None, lambda: None)
            for s in range(1, PASSES + 1):
                def row(r, parity, s=s):
                    first = static(r) and r == 0
                    g = bodies_before(s, r)
                    b = squares_before(s, r) if s >= 3 else 0
                    g = g if static(r) else pe.snap(g)
                    b = b if static(b) else pe.snap(b)
                    rb = place(pe, s, r)
                    done = BLOCKS * (s - 1) + r
                    if first:
                        pe.wait_ge(h_ready, BLOCKS * (s - 1) + (1 if s == 1 else BLOCKS))
                    if s == 1 and not first or s == 2 and first:
                        pe.wait_ge(acc_read, done)
                    elif s == PASSES and not first:
                        pe.wait_ge(y_ready, LINEAR[s] * BLOCKS + r - 1)
                    elif s > 1:
                        pe.wait_ge(acc_read, done - 1)
                    steps = nothing
                    if s in LINEAR and not first:
                        n = LINEAR[s] * BLOCKS + r - 1
                        steps = (lambda: turn(s, n), lambda: linear(s, n))
                    body(s, g, b, rb, parity, steps, True)
                    if s == 1 and not (static(r) and r == BLOCKS - 1):
                        with pe.Fori(r + 1, BLOCKS) as j:
                            if first:
                                pe.wait_ge(h_ready, j + 1)
                            body(s, (BLOCKS - 1) * r + j, 0, j, parity, None, True)
                    if not first:
                        with pe.Fori(0, r) as j:
                            jb = place(pe, s, j)
                            if s < PASSES:
                                pe.wait_ge(h_ready, BLOCKS * s + j + 1)
                            body(s, (BLOCKS - 1) * r + BLOCKS + j if s == 1 else g + 1 + j, b + j if s == 3 else b + 1 + j,
                                 jb, parity, None, s == PASSES)
                row_blocks(pe, row)
                if s in LINEAR:
                    turn(s, LINEAR[s] * BLOCKS + BLOCKS - 1)
                    linear(s, LINEAR[s] * BLOCKS + BLOCKS - 1)

        @block.scalar
        def _(act):
            act.dma_start(x[:, :, :], x_d).then_inc(x_loaded, 16)
            act.dma_start(partial[:, :, :], u_d).then_inc(u_loaded, 16)
            act.dma_start(w2[:, :], w2_d).then_inc(weights_loaded, 16)
            act.dma_start(wl[:, :, :], wl_d).then_inc(weights_loaded, 16)
            act.dma_start(eye[:, :], eye_d).then_inc(weights_loaded, 16)

            def root(n):
                act.wait_ge(var_ready, n + 1)
                nc.scalar.activation(std[:, :], var[:, :], ACT.Sqrt).then_inc(std_ready, 1)

            def square(g, b):
                for k in range(BT):
                    act.wait_ge(adj_loaded[k], 16 * g + 16)
                    act.wait_ge(sq_used, BT * b + k + 1)
                    nc.scalar.activation(sq[:, k, :], adj[:, k, :], ACT.Square).then_inc(squared, 1)

            with act.Fori(0, BLOCKS) as c:
                root(c)
            for s in range(1, PASSES + 1):
                def row(r, parity, s=s):
                    first = static(r) and r == 0
                    if s < SQUARED_FROM and not first:
                        root(BLOCKS * s + r - 1)
                    if s >= 3:
                        g, b = bodies_before(s, r), squares_before(s, r)
                        if not static(r):
                            g, b = act.snap(g), act.snap(b)
                        if s > 3:
                            square(g, b)
                        if not first:
                            with act.Fori(0, r) as j:
                                square(g + 1 + j, b + j if s == 3 else b + 1 + j)
                row_blocks(act, row)
                if s < SQUARED_FROM:
                    root(BLOCKS * s + BLOCKS - 1)

        @block.vector
        def _(dve):
            count = [0]

            def begin():
                dve.sem_clear(step)
                count[0] = 0

            def link(ins):
                count[0] += 1
                ins.then_inc(step, 1)
                dve.wait_ge(step, count[0])

            def wide(v):
                return v[:, :].unsqueeze(2).broadcast_to([P, BT, D])

            def norm(xb, n, hb, keep=None):
                link(nc.vector.tensor_reduce(rsum[:, :], xb, AX, ALU.add))
                link(nc.vector.tensor_scalar(mneg[:, :], rsum[:, :], -1.0 / D, None, ALU.mult))
                link(nc.vector.tensor_tensor(xc[:, :, :], xb, wide(mneg), ALU.add))
                link(nc.vector.tensor_tensor(xsq[:, :, :], xc[:, :, :], xc[:, :, :], ALU.mult))
                link(nc.vector.tensor_reduce(vsum[:, :], xsq[:, :, :], AX, ALU.add))
                nc.vector.tensor_scalar(var[:, :], vsum[:, :], 1.0 / D, EPS, ALU.mult, ALU.add).then_inc(var_ready, 1)
                dve.wait_ge(std_ready, n + 1)
                link(nc.vector.reciprocal(r0[:, :], std[:, :]))
                link(nc.vector.tensor_tensor(nt[:, :], r0[:, :], r0[:, :], ALU.mult))
                link(nc.vector.tensor_tensor(nt[:, :], nt[:, :], var[:, :], ALU.mult))
                link(nc.vector.tensor_scalar(nt[:, :], nt[:, :], -0.5, 1.5, ALU.mult, ALU.add))
                link(nc.vector.tensor_tensor(rstd[:, :], r0[:, :], nt[:, :], ALU.mult))
                if keep is None:
                    nc.vector.scalar_tensor_tensor(hb, xc[:, :, :], 0.0, wide(rstd), ALU.max,
                                                   ALU.mult).then_inc(h_ready, 1)
                    return
                link(nc.vector.scalar_tensor_tensor(xsq[:, :, :], xc[:, :, :], 0.0, wide(rstd), ALU.max, ALU.mult))
                link(nc.vector.tensor_scalar(xc[:, :, :], keep, KEEP_FROM, KEEP_SCALE, ALU.is_ge, ALU.mult))
                nc.vector.tensor_tensor(hb, xsq[:, :, :], xc[:, :, :], ALU.mult).then_inc(h_ready, 1)

            nc.vector.memset(h[:, :, 2 * D:HW], 1.0).then_inc(adj_used, BT)
            nc.vector.memset(ycat[:, :, D + 1:2 * D], 0.0).then_inc(squared, BT)
            nc.vector.memset(ycat[:, :, D:D + 1], 1.0).then_inc(sq_used, BT)
            nc.vector.memset(cat[:, :, :], 0.0).then_inc(consts_set, 1)

            dve.wait_ge(x_loaded, 16)
            dve.wait_ge(u_loaded, 16)
            with dve.Fori(0, BLOCKS) as c:
                begin()
                norm(x[:, bass.ds(c * BT, BT), :], c, h_two[1][:, bass.ds(c * BT, BT), :],
                     keep=partial[:, bass.ds(c * BT, BT), :])

            def finish(s, r, parity):
                first = static(r) and r == 0
                rb = place(dve, s, r)
                xb = x[:, bass.ds(rb * BT, BT), :]
                pb = partial[:, bass.ds(rb * BT, BT), :]
                own = h_two[s % 2][:, bass.ds(rb * BT, BT), :]
                nxt = h_two[(s + 1) % 2][:, bass.ds(rb * BT, BT), :]
                tiles = acc_tiles(s, parity)
                own_acc = tiles[:, :, (s % 2) * D:(s % 2) * D + D]
                nxt_acc = tiles[:, :, ((s + 1) % 2) * D:((s + 1) % 2) * D + D]
                begin()
                if s < 3 or s == 3 and first:
                    dve.wait_ge(adj_used, BT * bodies_before(s, r + 1) + BT)
                else:
                    dve.wait_ge(sq_used, BT * squares_before(s, r + 1) + BT)

                def keep_partial():
                    if s == PASSES:
                        return
                    if first:
                        nc.vector.memset(pb, 0.0).then_inc(acc_read, 1)
                    else:
                        nc.vector.tensor_scalar(pb, nxt_acc, 1.0, None, ALU.mult).then_inc(acc_read, 1)

                n = BLOCKS * s + r
                if s == DEG_PASS:
                    rd = rdeg[:, bass.ds(rb * BT, BT)]
                    link(nc.vector.tensor_tensor(xb, xb, own_acc, ALU.add))
                    link(nc.vector.tensor_scalar(nt[:, :].unsqueeze(2), tiles[:, :, 2 * D:2 * D + 1], 1.0, None, ALU.max))
                    keep_partial()
                    link(nc.vector.reciprocal(rd, nt[:, :]))
                    norm(xb, n, nxt)
                elif s == OUTER_PASS:
                    link(nc.vector.tensor_tensor(xc[:, :, :], own_acc, pb, ALU.add))
                    keep_partial()
                    link(nc.vector.tensor_tensor(xsq[:, :, :], xc[:, :, :], own, ALU.mult))
                    link(nc.vector.tensor_reduce(rsum[:, :], xsq[:, :, :], AX, ALU.add))
                    link(nc.vector.tensor_scalar(mneg[:, :], rsum[:, :], -0.01, 1.0, ALU.mult, ALU.add))
                    link(nc.vector.scalar_tensor_tensor(xb, own, -0.1, xb, ALU.mult, ALU.add))
                    link(nc.vector.tensor_tensor(xb, xb, wide(mneg), ALU.add))
                    norm(xb, n, nxt)
                else:
                    ln = LINEAR[s] * BLOCKS + r
                    if s == RELU_PASS:
                        rd = rdeg[:, bass.ds(rb * BT, BT)]
                        link(nc.vector.tensor_tensor(xc[:, :, :], own_acc, pb, ALU.add))
                        nc.vector.tensor_copy(cat[:, :, 0:D], own)
                        keep_partial()
                        nc.vector.tensor_tensor(cat[:, :, D:2 * D], xc[:, :, :],
                                                rd.unsqueeze(2).broadcast_to([P, BT, D]), ALU.mult).then_inc(y_ready, 1)
                    else:
                        nc.vector.tensor_tensor(ycat[:, :, 0:D], own_acc, pb, ALU.add).then_inc(y_ready, 1)
                        if s < PASSES:
                            dve.wait_ge(y_ready, ln + 1)
                            keep_partial()
                    dve.wait_ge(y_turned, ln + 1)
                    nc.vector.tensor_copy(lhs[:, :], turned[:, :]).then_inc(lhs_ready, 1)
                    dve.wait_ge(lin_done, ln + 1)
                    lint = lin[:, :].rearrange("p (t c) -> p t c", t=BT)
                    if s == RELU_PASS:
                        link(nc.vector.scalar_tensor_tensor(xb, lint, 0.0, xb, ALU.max, ALU.add))
                        norm(xb, n, nxt)
                    elif s < PASSES:
                        nc.vector.tensor_scalar(nxt, lint, 1.0, None, ALU.mult).then_inc(h_ready, 1)
                    else:
                        nc.vector.tensor_tensor(xb, lint, xb, ALU.add).then_inc(out_ready, 1)

            for s in range(1, PASSES + 1):
                row_blocks(dve, lambda r, parity, s=s: finish(s, r, parity))

        @block.gpsimd
        def _(pool):
            with pool.Fori(0, BLOCKS) as r:
                rb = place(pool, PASSES, r)
                pool.wait_ge(out_ready, r + 1)
                pool.dma_start(out_d[:, bass.ds(rb * BT, BT), :], x[:, bass.ds(rb * BT, BT), :]).then_inc(stored, 16)
            pool.wait_ge(stored, 16 * BLOCKS)


def kernel(x, adj, L0_gnn_u, L1_gnn_W, L2_gnn_t, L3_gnn_W0, L3_gnn_b0, L3_gnn_W1, L3_gnn_b1, L3_gnn_W2, L3_gnn_b2):
    import numpy as np
    import concourse.bacc as bacc
    from concourse.bass_utils import run_bass_kernel_spmd

    def rows_on_partitions(a):
        return np.ascontiguousarray(np.asarray(a).reshape(TILES, P, D).transpose(1, 0, 2))

    weights = [(L3_gnn_W0, L3_gnn_b0), (L3_gnn_W1, L3_gnn_b1), (L3_gnn_W2, L3_gnn_b2)]
    arrays = {
        "x_in": rows_on_partitions(x),
        "adj_in": np.ascontiguousarray(np.asarray(adj).reshape(BLOCKS, BLOCK, TILES, P).transpose(0, 2, 3, 1)).reshape(
            BLOCKS * TILES, P, BLOCK),
        "u_in": rows_on_partitions(L0_gnn_u),
        "w2_in": np.ascontiguousarray(np.asarray(L1_gnn_W).T),
        "wl_in": np.ascontiguousarray(np.stack([np.concatenate([np.asarray(w).T, np.asarray(b)[None, :]], axis=0)
                                                for w, b in weights], axis=1)),
        "eye_in": np.eye(P, dtype=np.float32),
    }
    nc = bacc.Bacc("TRN2", target_bir_lowering=False, num_devices=1)
    aps = [nc.dram_tensor(name, a.shape, mybir.dt.from_np(a.dtype), kind="ExternalInput").ap()
           for name, a in arrays.items()]
    out = nc.dram_tensor("out", (P, TILES, D), F32, kind="ExternalOutput").ap()
    build(nc, *aps, out)
    r = run_bass_kernel_spmd(nc, [arrays], core_ids=[0])
    return np.ascontiguousarray(r.results[0]["out"].transpose(1, 0, 2)).reshape(N, D)
```

```python
from contextlib import ExitStack

import concourse.bass as bass
from concourse import mybir

P = 128
N = 8192
D = 64
TILES = N // P
BT = 8
BLOCK = BT * P
BLOCKS = N // BLOCK
ST = 4
CHUNK = 512
PASSES = 6
LINEAR = {2: 0, 4: 1, 5: 2, 6: 3}
NORM = {1: 0, 2: 1, 3: 2}
DIRECT = (3, 7)
SPLIT = [k for k in range(BT) if k not in DIRECT]
KEEP_FROM = 0.1
KEEP_SCALE = 1.0 / 0.9
EPS = 1e-5
TURN_H_AT, PE_AT = 0, 2
TAKE_AT, MIDDLE_AT, END_AT = 3, 4, 5

ALU = mybir.AluOpType
ACT = mybir.ActivationFunctionType
AX = mybir.AxisListType.X
F32 = mybir.dt.float32
F32R = mybir.dt.float32r



def bodies_before(s, r):
    if s == 1:
        return BLOCKS * r
    return BLOCKS * BLOCKS + (s - 2) * (BLOCKS * (BLOCKS + 1) // 2) + r * (r + 1) // 2


def squares_before(s, r):
    if s == 3:
        return r * (r - 1) // 2
    return BLOCKS * (BLOCKS - 1) // 2 + (s - 4) * (BLOCKS * (BLOCKS + 1) // 2) + r * (r + 1) // 2


def square_splits_before(s, r):
    return (s - 4) * (BLOCKS * (BLOCKS + 1) // 2) + r * (r + 1) // 2


def static(r):
    return isinstance(r, int)


def in_register(eng, value, top=1 << 14):
    if static(value):
        return value
    return eng.snap(eng.to_reg(value), donate=True, min_val=0, max_val=top)


def place(eng, s, r):
    return r if s % 2 else in_register(eng, BLOCKS - 1 - r, BLOCKS - 1)


def row_blocks(eng, row):
    row(0, 0)
    with eng.Fori(0, BLOCKS // 2 - 1) as i:
        row(eng.snap(2 * i + 1), 1)
        row(eng.snap(2 * i + 2), 0)
    row(BLOCKS - 1, 1)


class Body:

    def __init__(self, s, g, b, c, rb, jb, j, paired, corner):
        self.s, self.rb, self.jb, self.j, self.paired, self.corner = s, rb, jb, j, paired, corner
        self.loaded = g
        self.squared = b
        self.split = c


def bodies(eng, s, r, run):
    g = bodies_before(s, r)
    b = squares_before(s, r) if s >= 3 else 0
    c = square_splits_before(s, r) if s >= 4 else 0
    g, b, c = [v if static(v) else eng.snap(v) for v in (g, b, c)]
    rb = place(eng, s, r)
    run(Body(s, g, b, c, rb, rb, r, False, True))
    if s == 1 and not (static(r) and r == BLOCKS - 1):
        with eng.Fori(r + 1, BLOCKS) as j:
            run(Body(s, (BLOCKS - 1) * r + j, 0, 0, rb, j, j, False, False))
    if not (static(r) and r == 0):
        with eng.Fori(0, r) as j:
            jb = place(eng, s, j)
            run(Body(s, (BLOCKS - 1) * r + BLOCKS + j if s == 1 else g + 1 + j,
                     b + j if s == 3 else b + 1 + j, c + 1 + j, rb, jb, j, s < PASSES, False))


def half(s):
    return slice(0, D) if s % 2 else slice(D, 2 * D)


def build(nc, x_d, adj_d, u_d, w2_d, wl_d, eye_d, out_d):
    with ExitStack() as ctx:
        def sb(name, shape, dt=F32):
            return ctx.enter_context(nc.sbuf_tensor(name, shape, dt))

        def sem(name):
            return ctx.enter_context(nc.semaphore(name))

        adj = sb("adj", [P, BT, BLOCK])
        hi = sb("hi", [P, BT, BLOCK], F32R)
        lo = sb("lo", [P, BT, BLOCK], F32R)
        h = sb("h", [P, TILES, 2 * D])
        x = sb("x", [P, TILES, D])
        partial = sb("partial", [P, N])
        stat_two = sb("stat_two", [P, ST, 2, P], F32R)
        stat_one = sb("stat_one", [P, ST, 2, P], F32R)
        stat_raw = sb("stat_raw", [P, ST, P])
        tall = sb("tall", [P, BLOCK])
        lhs = sb("lhs", [P, BLOCK])
        w2 = sb("w2", [P, D])
        wl = sb("wl", [D + 1, 3, D])
        eye = sb("eye", [P, P])
        ones = sb("ones", [P, P], F32R)
        zeros = sb("zeros", [P, P], F32R)
        xc = sb("xc", [P, BT, D])
        xsq = sb("xsq", [P, BT, D])
        degree_sum = lhs[0:D, :]
        rsum, mneg, vsum, var, std, r0, nt, rstd = [
            sb(name, [P, BT]) for name in ("rsum", "mneg", "vsum", "var", "std", "r0", "nt", "rstd")]

        ps = ctx.enter_context(nc.psum_tensor("ps", [P, 8 * CHUNK], F32))
        acc = [ps[:, 0:BLOCK], ps[:, BLOCK:2 * BLOCK]]
        one_acc, two_acc = acc
        degree = ps[:, 2 * BLOCK:3 * BLOCK]
        lin = ps[:, 2 * BLOCK:2 * BLOCK + CHUNK]
        turned = ps[:, 3 * BLOCK:4 * BLOCK]

        adj_loaded = [sem(f"adj_loaded{k}") for k in range(BT)]
        x_loaded = sem("x_loaded")
        u_loaded = sem("u_loaded")
        weights_loaded = sem("weights_loaded")
        used = sem("used")
        copied = sem("copied")
        split = sem("split")
        squared = sem("squared")
        square_hi = sem("square_hi")
        square_split = sem("square_split")
        staged = sem("staged")
        stage_step = sem("stage_step")
        acc_taken_act = sem("acc_taken_act")
        acc_taken_dve = sem("acc_taken_dve")
        tall_half = sem("tall_half")
        tall_ready = sem("tall_ready")
        h_copied = sem("h_copied")
        h_turned = sem("h_turned")
        tall_turned = sem("tall_turned")
        lhs_ready = sem("lhs_ready")
        lin_done = sem("lin_done")
        h_ready = sem("h_ready")
        degree_ready = sem("degree_ready")
        var_ready = sem("var_ready")
        std_ready = sem("std_ready")
        step = sem("step")
        out_ready = sem("out_ready")
        stored = sem("stored")

        def row_done(s, r):
            return BT * bodies_before(s, r + 1) + BT

        def cols(rb):
            return bass.ds(rb * BLOCK, BLOCK)

        def before(s, r):
            if static(r) and r == 0:
                return (s - 1, BLOCKS - 1, 1)
            return (s, r - 1, None)

        block = ctx.enter_context(nc.Block())

        @block.sync
        def _(sp):
            def load(o):
                for k in range(BT):
                    tile = in_register(sp, o.rb * TILES + o.jb * BT + k, BLOCKS * TILES - 1)
                    free = BT * o.loaded + k + 1
                    if o.s <= 2:
                        sp.wait_ge(split, free)
                    elif o.s == 3 or o.s == 4 and static(o.j) and o.j == 0 and o.corner or k in DIRECT:
                        sp.wait_ge(used, free)
                    else:
                        sp.wait_ge(square_split, len(SPLIT) * o.split + SPLIT.index(k) + 1)
                    sp.dma_start(adj[:, k, :], adj_d[tile]).then_inc(adj_loaded[k], 16)

            for s in range(1, PASSES + 1):
                row_blocks(sp, lambda r, parity, s=s: bodies(sp, s, r, load))

        @block.gpsimd
        def _(pool):
            def stage(o):
                s, own = o.s, half(o.s)
                pool.sem_clear(stage_step)
                if s == 1 and not o.paired:
                    if static(o.rb) and o.rb == 0:
                        pool.wait_ge(h_ready, o.j + 1)
                elif o.corner and static(o.j) and o.j == 0:
                    pool.wait_ge(h_ready, BLOCKS * s)
                elif o.paired:
                    pool.wait_ge(h_ready, BLOCKS * s + o.j + 1)
                steps = 0
                for k in range(BT):
                    pool.wait_ge(used, BT * o.loaded + BT - ST + k + 1)
                    tile = h[:, bass.ds(o.jb * BT + k, 1), :].rearrange("p a c -> p (a c)")
                    if s >= 4 and k in DIRECT:
                        nc.gpsimd.tensor_copy(stat_raw[:, k % ST, :] if o.paired else stat_raw[:, k % ST, own],
                                              tile if o.paired else tile[:, own]).then_inc(staged, 1)
                        continue
                    if s == 3:
                        src, a, b = tile[:, own], stat_two[:, k % ST, 0, 0:D], stat_two[:, k % ST, 0, D:2 * D]
                    elif o.paired:
                        src, a, b = tile, stat_two[:, k % ST, 0, :], stat_two[:, k % ST, 1, :]
                    else:
                        src, a, b = tile[:, own], stat_one[:, k % ST, 0, own], stat_one[:, k % ST, 1, own]
                    nc.gpsimd.tensor_copy(a, src).then_inc(stage_step, 1)
                    steps += 1
                    if s == 3 and o.paired:
                        nc.gpsimd.tensor_copy(stat_raw[:, k % ST, :], tile).then_inc(stage_step, 1)
                        steps += 1
                    pool.wait_ge(stage_step, steps)
                    nc.gpsimd.tensor_tensor(b, src, a.bitcast(F32), ALU.subtract).then_inc(staged, 1)

            def fill(half_tiles, value):
                nc.gpsimd.memset(half_tiles.bitcast(F32), value).then_inc(stage_step, 1)

            for s in range(1, PASSES + 1):
                if s in (1, 2, 5, 6):
                    pool.sem_clear(stage_step)
                    other = half(s + 1)
                    if s > 1:
                        pool.wait_ge(used, row_done(s - 1, BLOCKS - 1))
                    fill(stat_one[:, :, 0, other], 1.0 if s == 1 else 0.0)
                    fill(stat_one[:, :, 1, other], 0.0)
                    pool.wait_ge(stage_step, 2)
                row_blocks(pool, lambda r, parity, s=s: bodies(pool, s, r, stage))
            for r in range(BLOCKS):
                rb = place(pool, PASSES, r)
                pool.wait_ge(out_ready, r + 1)
                pool.dma_start(out_d[:, rb * BT:rb * BT + BT, :], x[:, rb * BT:rb * BT + BT, :]).then_inc(stored, 16)
            pool.wait_ge(stored, 16 * BLOCKS)

        @block.tensor
        def _(pe):
            def products(out, st, k, moving, start=False):
                for m in moving:
                    for c in range(0, BLOCK, CHUNK):
                        last = nc.tensor.matmul(out[:, c:c + CHUNK], st, m[:, k, c:c + CHUNK], start=start, stop=False,
                                                skip_group_check=True)
                    start = False
                return last

            def clear(out, whole):
                for c in range(0, BLOCK, P if whole else CHUNK):
                    nc.tensor.matmul(out[:, c:c + P], zeros[:, :], zeros[:, :], start=c % CHUNK == 0, stop=False,
                                     skip_group_check=True)

            def multiply(o, parity, steps):
                s, own = o.s, half(o.s)
                for k in range(BT):
                    pe.wait_ge(staged, BT * o.loaded + k + 1)
                    start = o.corner and k == 0
                    if s <= 3:
                        pe.wait_ge(split, BT * o.loaded + BT + k + 1)
                    elif k in DIRECT:
                        pe.wait_ge(squared, BT * o.squared + k + 1)
                    else:
                        pe.wait_ge(square_split, len(SPLIT) * o.split + len(SPLIT) + SPLIT.index(k) + 1)
                    if s == 3:
                        last = products(one_acc, stat_two[:, k % ST, 0, :], k, (hi, lo), start)
                        if o.paired:
                            pe.wait_ge(squared, BT * o.squared + k + 1)
                            last = products(two_acc, stat_raw[:, k % ST, :], k, (adj,))
                    elif s >= 4 and k in DIRECT:
                        if o.paired:
                            last = products(acc[parity], stat_raw[:, k % ST, :], k, (adj,))
                        else:
                            last = products(acc[parity][own, :], stat_raw[:, k % ST, own], k, (adj,))
                    else:
                        out = acc[parity] if s > 1 else two_acc if o.paired else one_acc
                        st = stat_two if o.paired else stat_one
                        products(out, st[:, k % ST, 0, :], k, (hi, lo), start)
                        last = products(out, st[:, k % ST, 1, :], k, (hi,))
                        if s == 1 and o.paired:
                            last = products(degree, ones[:, :], k, (hi, lo))
                    last.then_inc(used, 1)
                    for do in steps.get(k, ()):
                        do()

            def turn_h(r):
                pe.wait_ge(h_copied, r + 1)
                pe.wait_ge(tall_half, BLOCKS + r)
                for t in range(BT):
                    last = nc.tensor.transpose(turned[:, t * P:(t + 1) * P], lhs[:, t * P:(t + 1) * P], eye[:, :])
                last.then_inc(h_turned, 1)

            def turn_sums(s, r):
                if s == 1:
                    pe.wait_ge(tall_ready, r + 1)
                else:
                    pe.wait_ge(acc_taken_dve, 2 * BLOCKS + r + 1)
                    pe.wait_ge(tall_half, 2 * BLOCKS + r + 1)
                for t in range(BT):
                    last = nc.tensor.transpose(turned[:, t * P:(t + 1) * P], tall[:, t * P:(t + 1) * P], eye[:, :])
                last.then_inc(tall_turned, 1)

            def linear(s, r):
                w = w2[:, :] if s == 2 else wl[:, LINEAR[s] - 1, :]
                src = tall[:, :] if s == 2 else lhs[0:D + 1, :]
                if s > 2:
                    pe.wait_ge(acc_taken_dve, BLOCKS * (s - 1) + r + 1)
                else:
                    pe.wait_ge(lhs_ready, r + 1)
                    pe.wait_ge(tall_half, BLOCKS + r + 1)
                for t in range(BT):
                    last = nc.tensor.matmul(lin[:, t * D:(t + 1) * D], src[:, t * P:(t + 1) * P], w, start=True, stop=True)
                last.then_inc(lin_done, 1)

            def steps_behind(s, r):
                if s in (1, 3):
                    return {PE_AT: [lambda: turn_sums(s, r)]}
                if s == 2:
                    return {TURN_H_AT: [lambda: turn_h(r)], PE_AT: [lambda: linear(s, r)]}
                return {PE_AT: [lambda: linear(s, r)]}

            pe.wait_ge(used, BT)
            pe.wait_ge(split, BT)
            pe.wait_ge(weights_loaded, 48)
            for s in range(1, PASSES + 1):
                def row(r, parity, s=s):
                    first = static(r) and r == 0
                    rows = BLOCKS * (s - 1) + r
                    if s > 1 or not first:
                        ago = 0 if s in (1, 3) or first else 1
                        pe.wait_ge(acc_taken_dve, rows - ago)
                        if s not in (2, 3, PASSES) or first and s != 3:
                            pe.wait_ge(acc_taken_act, rows - ago - (BLOCKS if s > 2 else 0))
                        elif s == 3 and not first:
                            pe.wait_ge(acc_taken_act, BLOCKS + r)
                    if s in (1, 3):
                        clear(two_acc, first)
                    if s == 1:
                        clear(degree, first)
                    behind = {} if first else steps_behind(*before(s, r)[:2])
                    bodies(pe, s, r, lambda o: multiply(o, parity, behind if o.corner else {}))
                row_blocks(pe, row)
                for do in [do for _, dos in sorted(steps_behind(s, BLOCKS - 1).items()) for do in dos]:
                    do()

        @block.scalar
        def _(act):
            act.dma_start(x[:, :, :], x_d).then_inc(x_loaded, 16)
            act.dma_start(partial[:, 0:TILES * D].rearrange("p (t d) -> p t d", d=D), u_d).then_inc(u_loaded, 16)
            act.dma_start(w2[:, :], w2_d).then_inc(weights_loaded, 16)
            act.dma_start(wl[:, :, :], wl_d).then_inc(weights_loaded, 16)
            act.dma_start(eye[:, :], eye_d).then_inc(weights_loaded, 16)

            def root(n):
                act.wait_ge(var_ready, n + 1)
                nc.scalar.activation(std[:, :], var[:, :], ACT.Sqrt).then_inc(std_ready, 1)

            def square(o, k):
                nc.scalar.activation(adj[:, k, :], adj[:, k, :], ACT.Square).then_inc(squared, 1)

            def square_behind(o, k):
                act.wait_ge(split, BT * o.loaded + BT + k + 1)
                square(o, k)

            def prepare(o, steps):
                s = o.s
                if s == 1 and static(o.rb) and o.rb == 0:
                    root(o.j)
                for k in range(BT):
                    act.wait_ge(adj_loaded[k], 16 * o.loaded + 16)
                    if s <= 3:
                        act.wait_ge(used, BT * o.loaded + k + 1)
                        nc.scalar.activation(hi[:, k, :], adj[:, k, :], ACT.Copy).then_inc(copied, 1)
                        if s == 3 and o.paired and k >= 1:
                            square_behind(o, k - 1)
                    else:
                        square(o, k)
                    for do in steps.get(k, ()):
                        do()
                if s == 3 and o.paired:
                    square_behind(o, BT - 1)

            def take(s, r, parity):
                rb = place(act, s, r)
                done = in_register(act, row_done(s, r))
                to = partial[half(s + 1), cols(rb)]
                n = (BLOCKS if s == 2 else 2 * BLOCKS) + r
                if s == 2:
                    act.wait_ge(h_turned, r + 1)
                    nc.scalar.activation(tall[D:2 * D, :], turned[D:2 * D, :], ACT.Copy).then_inc(tall_half, 1)
                    return
                act.wait_ge(used, done)
                if s == 1:
                    nc.scalar.activation(tall[:, :], one_acc, ACT.Copy).then_inc(tall_half, 1)
                    nc.scalar.activation(to, two_acc[half(2), :], ACT.Copy).then_inc(acc_taken_act, 1)
                elif s == 3:
                    nc.scalar.activation(tall[D:2 * D, :], one_acc[D:2 * D, :], ACT.Copy).then_inc(tall_half, 1)
                    nc.scalar.activation(to, two_acc[half(4), :], ACT.Copy).then_inc(acc_taken_act, 1)
                elif s < PASSES:
                    nc.scalar.activation(to, acc[parity][half(s + 1), :], ACT.Copy).then_inc(acc_taken_act, 1)

            def copy_h(r):
                rb = place(act, 2, r)
                act.wait_ge(h_ready, 2 * BLOCKS)
                act.wait_ge(degree_ready, BLOCKS)
                act.wait_ge(tall_half, BLOCKS + r)
                nc.scalar.activation(lhs[:, :].rearrange("p (t c) -> p t c", t=BT), h[:, bass.ds(rb * BT, BT), :],
                                     ACT.Copy).then_inc(h_copied, 1)

            def steps_behind(s, r, parity):
                steps = {TAKE_AT: [lambda: take(s, r, parity)]}
                if s == 2:
                    steps[TURN_H_AT] = [lambda: copy_h(r)]
                if s in NORM:
                    steps[END_AT] = [lambda: root(BLOCKS * (1 + NORM[s]) + r)]
                return steps

            for s in range(1, PASSES + 1):
                def row(r, parity, s=s):
                    behind = {}
                    if s > 1 or not (static(r) and r == 0):
                        behind = steps_behind(*before(s, r)[:2], 1 - parity)
                    bodies(act, s, r, lambda o: prepare(o, behind if o.corner else {}))
                row_blocks(act, row)

        @block.vector
        def _(dve):
            count = [0]

            def begin():
                dve.sem_clear(step)
                count[0] = 0

            def link(ins):
                count[0] += 1
                ins.then_inc(step, 1)
                dve.wait_ge(step, count[0])

            def wide(v):
                return v[:, :].unsqueeze(2).broadcast_to([P, BT, D])

            def norm_begin(xb):
                link(nc.vector.tensor_reduce(rsum[:, :], xb, AX, ALU.add))
                link(nc.vector.tensor_scalar(mneg[:, :], rsum[:, :], -1.0 / D, None, ALU.mult))
                link(nc.vector.tensor_tensor(xc[:, :, :], xb, wide(mneg), ALU.add))
                link(nc.vector.tensor_tensor(xsq[:, :, :], xc[:, :, :], xc[:, :, :], ALU.mult))
                link(nc.vector.tensor_reduce(vsum[:, :], xsq[:, :, :], AX, ALU.add))
                nc.vector.tensor_scalar(var[:, :], vsum[:, :], 1.0 / D, EPS, ALU.mult, ALU.add).then_inc(var_ready, 1)

            def norm_end(n, hb, keep=None):
                dve.wait_ge(std_ready, n + 1)
                link(nc.vector.reciprocal(r0[:, :], std[:, :]))
                link(nc.vector.tensor_tensor(nt[:, :], r0[:, :], r0[:, :], ALU.mult))
                link(nc.vector.tensor_tensor(nt[:, :], nt[:, :], var[:, :], ALU.mult))
                link(nc.vector.tensor_scalar(nt[:, :], nt[:, :], -0.5, 1.5, ALU.mult, ALU.add))
                link(nc.vector.tensor_tensor(rstd[:, :], r0[:, :], nt[:, :], ALU.mult))
                if keep is None:
                    nc.vector.scalar_tensor_tensor(hb, xc[:, :, :], 0.0, wide(rstd), ALU.max,
                                                   ALU.mult).then_inc(h_ready, 1)
                    return
                link(nc.vector.scalar_tensor_tensor(xsq[:, :, :], xc[:, :, :], 0.0, wide(rstd), ALU.max, ALU.mult))
                link(nc.vector.tensor_scalar(xc[:, :, :], keep, KEEP_FROM, KEEP_SCALE, ALU.is_ge, ALU.mult))
                nc.vector.tensor_tensor(hb, xsq[:, :, :], xc[:, :, :], ALU.mult).then_inc(h_ready, 1)

            nc.vector.memset(zeros[:, :].bitcast(F32), 0.0).then_inc(used, BT)
            nc.vector.memset(ones[:, :].bitcast(F32), 1.0).then_inc(split, BT)
            nc.vector.memset(rsum[:, :], 0.0).then_inc(square_split, len(SPLIT))
            dve.wait_ge(square_split, len(SPLIT))
            dve.wait_ge(x_loaded, 16)
            dve.wait_ge(u_loaded, 16)

            def prepare(o, steps):
                s = o.s
                if s == 1 and static(o.rb) and o.rb == 0:
                    begin()
                    norm_begin(x[:, bass.ds(o.j * BT, BT), :])
                    norm_end(o.j, h[:, bass.ds(o.j * BT, BT), half(1)],
                             keep=partial[:, bass.ds(o.j * BT * D, BT * D)].rearrange("p (t d) -> p t d", d=D))
                for k in range(BT):
                    if s <= 3:
                        dve.wait_ge(copied, BT * o.loaded + k + 1)
                        nc.vector.tensor_tensor(lo[:, k, :], adj[:, k, :], hi[:, k, :].bitcast(F32),
                                                ALU.subtract).then_inc(split, 1)
                    elif k in SPLIT:
                        n = len(SPLIT) * o.split + SPLIT.index(k) + 1
                        dve.wait_ge(squared, BT * o.squared + k + 1)
                        dve.wait_ge(used, BT * o.loaded + k + 1)
                        nc.vector.tensor_scalar(hi[:, k, :], adj[:, k, :], 1.0, None, ALU.mult).then_inc(square_hi, 1)
                        dve.wait_ge(square_hi, n)
                        nc.vector.tensor_tensor(lo[:, k, :], adj[:, k, :], hi[:, k, :].bitcast(F32),
                                                ALU.subtract).then_inc(square_split, 1)
                    for do in steps.get(k, ()):
                        do()

            def steps_behind(s, r, parity):
                def names():
                    rb = place(dve, s, r)
                    tiles = bass.ds(rb * BT, BT)
                    return rb, x[:, tiles, :], h[:, tiles, half(s)], h[:, tiles, half(s + 1)]

                def take():
                    rb = place(dve, s, r)
                    own = partial[half(s), cols(rb)]
                    begin()
                    dve.wait_ge(used, row_done(s, r))
                    if s == 1:
                        dve.wait_ge(tall_half, r + 1)
                        nc.vector.tensor_tensor(tall[0:D, :], tall[0:D, :], two_acc[0:D, :],
                                                ALU.add).then_inc(tall_ready, 1)
                        nc.vector.tensor_tensor(degree_sum, tall[D:2 * D, :], degree[D:2 * D, :],
                                                ALU.add).then_inc(acc_taken_dve, 1)
                    elif s == 2:
                        dve.wait_ge(degree_ready, BLOCKS)
                        link(nc.vector.tensor_tensor(tall[0:D, :], acc[parity][half(2), :], own, ALU.add))
                        nc.vector.tensor_tensor(tall[0:D, :], tall[0:D, :], partial[0:D, cols(rb)],
                                                ALU.mult).then_inc(lhs_ready, 1)
                        dve.wait_ge(lhs_ready, r + 1)
                        nc.vector.tensor_scalar(partial[half(3), cols(rb)], acc[parity][half(3), :], 1.0, None,
                                                ALU.mult).then_inc(acc_taken_dve, 1)
                    elif s == 3:
                        if static(r):
                            dve.wait_ge(h_turned, BLOCKS)
                            link(nc.vector.memset(lhs[D:D + 1, :], 1.0))
                        nc.vector.tensor_tensor(tall[0:D, :], one_acc[0:D, :], own, ALU.add).then_inc(acc_taken_dve, 1)
                    else:
                        nc.vector.tensor_tensor(lhs[0:D, :], acc[parity][half(s), :], own,
                                                ALU.add).then_inc(acc_taken_dve, 1)

                def middle():
                    rb, xb, own, nxt = names()
                    sums = turned.rearrange("p (t c) -> p t c", t=BT)
                    lint = lin.rearrange("p (t c) -> p t c", t=BT)
                    if s == 1:
                        dve.wait_ge(tall_turned, r + 1)
                        link(nc.vector.tensor_tensor(xb, sums[:, :, 0:D], xb, ALU.add))
                        norm_begin(xb)
                    elif s == 2:
                        dve.wait_ge(lin_done, r + 1)
                        link(nc.vector.scalar_tensor_tensor(xb, lint, 0.0, xb, ALU.max, ALU.add))
                        norm_begin(xb)
                    elif s == 3:
                        dve.wait_ge(tall_turned, BLOCKS + r + 1)
                        link(nc.vector.tensor_reduce(xc[:, :, :], turned.rearrange("p (t a c) -> p t c a", t=BT, a=2),
                                                     AX, ALU.add))
                        link(nc.vector.tensor_tensor(xsq[:, :, :], xc[:, :, :], own, ALU.mult))
                        link(nc.vector.tensor_reduce(rsum[:, :], xsq[:, :, :], AX, ALU.add))
                        link(nc.vector.tensor_scalar(mneg[:, :], rsum[:, :], -0.01, 1.0, ALU.mult, ALU.add))
                        link(nc.vector.scalar_tensor_tensor(xb, own, -0.1, xb, ALU.mult, ALU.add))
                        link(nc.vector.tensor_tensor(xb, xb, wide(mneg), ALU.add))
                        norm_begin(xb)
                    elif s < PASSES:
                        dve.wait_ge(lin_done, LINEAR[s] * BLOCKS + r + 1)
                        nc.vector.tensor_scalar(nxt, lint, 1.0, None, ALU.mult).then_inc(h_ready, 1)
                    else:
                        dve.wait_ge(lin_done, LINEAR[s] * BLOCKS + r + 1)
                        nc.vector.tensor_tensor(xb, lint, xb, ALU.add).then_inc(out_ready, 1)

                def end():
                    rb, xb, own, nxt = names()
                    norm_end(BLOCKS * (1 + NORM[s]) + r, nxt)
                    if s == 1:
                        dve.wait_ge(acc_taken_dve, r + 1)
                        link(nc.vector.tensor_scalar(degree_sum, degree_sum, 1.0, None, ALU.max))
                        nc.vector.reciprocal(partial[0:D, cols(rb)], degree_sum).then_inc(degree_ready, 1)

                steps = {TAKE_AT: [take], MIDDLE_AT: [middle]}
                if s in NORM:
                    steps[END_AT] = [end]
                return steps

            for s in range(1, PASSES + 1):
                def row(r, parity, s=s):
                    behind = {}
                    if s > 1 or not (static(r) and r == 0):
                        behind = steps_behind(*before(s, r)[:2], 1 - parity)
                    bodies(dve, s, r, lambda o: prepare(o, behind if o.corner else {}))
                row_blocks(dve, row)
            for _, dos in sorted(steps_behind(PASSES, BLOCKS - 1, 1).items()):
                for do in dos:
                    do()


def kernel(x, adj, L0_gnn_u, L1_gnn_W, L2_gnn_t, L3_gnn_W0, L3_gnn_b0, L3_gnn_W1, L3_gnn_b1, L3_gnn_W2, L3_gnn_b2):
    import numpy as np
    import concourse.bacc as bacc
    from concourse.bass_utils import run_bass_kernel_spmd

    def rows_on_partitions(a):
        return np.ascontiguousarray(np.asarray(a).reshape(TILES, P, D).transpose(1, 0, 2))

    weights = [(L3_gnn_W0, L3_gnn_b0), (L3_gnn_W1, L3_gnn_b1), (L3_gnn_W2, L3_gnn_b2)]
    arrays = {
        "x_in": rows_on_partitions(x),
        "adj_in": np.ascontiguousarray(np.asarray(adj).reshape(BLOCKS, BLOCK, TILES, P).transpose(0, 2, 3, 1)).reshape(
            BLOCKS * TILES, P, BLOCK),
        "u_in": rows_on_partitions(L0_gnn_u),
        "w2_in": np.ascontiguousarray(np.roll(np.asarray(L1_gnn_W).T, D, axis=0)),
        "wl_in": np.ascontiguousarray(np.stack([np.concatenate([np.asarray(w).T, np.asarray(b)[None, :]], axis=0)
                                                for w, b in weights], axis=1)),
        "eye_in": np.eye(P, dtype=np.float32),
    }
    nc = bacc.Bacc("TRN2", target_bir_lowering=False, num_devices=1)
    aps = [nc.dram_tensor(name, a.shape, mybir.dt.from_np(a.dtype), kind="ExternalInput").ap()
           for name, a in arrays.items()]
    out = nc.dram_tensor("out", (P, TILES, D), F32, kind="ExternalOutput").ap()
    build(nc, *aps, out)
    r = run_bass_kernel_spmd(nc, [arrays], core_ids=[0])
    return np.ascontiguousarray(r.results[0]["out"].transpose(1, 0, 2)).reshape(N, D)
```

```python
from contextlib import ExitStack

import concourse.bass as bass
from concourse import mybir

P = 128
N = 8192
D = 64
TILES = N // P
BT = 8
BLOCK = BT * P
BLOCKS = N // BLOCK
SUMS_POOL = (4, 7)
SUMS_DVE = (1, 3, 5)
ST = 4
CHUNK = 512
PASSES = 6
LINEAR = {2: 0, 4: 1, 5: 2, 6: 3}
NORM = {1: 0, 2: 1, 3: 2}
DIRECT = (3, 7)
SPLIT = [k for k in range(BT) if k not in DIRECT]
DIRECT_FIRST = (2, 4, 6)
SPLIT_TWICE = (0, 2, 4, 5)
SQUARE_LAG = 2
TWICE_LAG = 2
KEEP_FROM = 0.1
KEEP_SCALE = 1.0 / 0.9
EPS = 1e-5
TURN_H_AT, PE_AT = 0, 1
STEPS_AT = {1: (5, 6, 7), 2: (3, 4, 5), 3: (4, 5, 7), 4: (3, 4, 5), 5: (3, 4, 5), 6: (3, 4, 5)}

ALU = mybir.AluOpType
ACT = mybir.ActivationFunctionType
AX = mybir.AxisListType.X
F32 = mybir.dt.float32
F32R = mybir.dt.float32r



def bodies_before(s, r):
    if s == 1:
        return BLOCKS * r
    return BLOCKS * BLOCKS + (s - 2) * (BLOCKS * (BLOCKS + 1) // 2) + r * (r + 1) // 2


def squares_before(s, r):
    if s == 3:
        return r * (r - 1) // 2
    return BLOCKS * (BLOCKS - 1) // 2 + (s - 4) * (BLOCKS * (BLOCKS + 1) // 2) + r * (r + 1) // 2


def square_splits_before(s, r):
    return (s - 4) * (BLOCKS * (BLOCKS + 1) // 2) + r * (r + 1) // 2


def paired_before(r):
    return r * (r - 1) // 2


def static(r):
    return isinstance(r, int)


def in_register(eng, value, top=1 << 14):
    if static(value):
        return value
    return eng.snap(eng.to_reg(value), donate=True, min_val=0, max_val=top)


def place(eng, s, r):
    return r if s % 2 else in_register(eng, BLOCKS - 1 - r, BLOCKS - 1)


def row_blocks(eng, row):
    row(0, 0)
    with eng.Fori(0, BLOCKS // 2 - 1) as i:
        row(eng.snap(2 * i + 1), 1)
        row(eng.snap(2 * i + 2), 0)
    row(BLOCKS - 1, 1)


class Body:

    def __init__(self, s, g, b, c, q, rb, jb, j, paired, corner):
        self.s, self.rb, self.jb, self.j, self.paired, self.corner = s, rb, jb, j, paired, corner
        self.loaded = g
        self.squared = b
        self.split = c
        self.summed = q
        self.first = s == 1 and static(rb) and rb == 0

    def counts(self, k):
        return 2 if self.first and k - 1 in DIRECT_FIRST else 1


def bodies(eng, s, r, run):
    g = bodies_before(s, r)
    b = squares_before(s, r) if s >= 3 else 0
    c = square_splits_before(s, r) if s >= 4 else 0
    q = paired_before(r) if s == 1 else 0
    g, b, c, q = [v if static(v) else eng.snap(v) for v in (g, b, c, q)]
    rb = place(eng, s, r)
    run(Body(s, g, b, c, q, rb, rb, r, False, True))
    if s == 1 and not (static(r) and r == BLOCKS - 1):
        with eng.Fori(r + 1, BLOCKS) as j:
            run(Body(s, (BLOCKS - 1) * r + j, 0, 0, q, rb, j, j, False, False))
    if not (static(r) and r == 0):
        with eng.Fori(0, r) as j:
            jb = place(eng, s, j)
            run(Body(s, (BLOCKS - 1) * r + BLOCKS + j if s == 1 else g + 1 + j,
                     b + j if s == 3 else b + 1 + j, c + 1 + j, q + j if s == 1 else 0, rb, jb, j, s < PASSES, False))


def half(s):
    return slice(0, D) if s % 2 else slice(D, 2 * D)


def build(nc, x_d, adj_d, u_d, w2_d, wl_d, eye_d, out_d):
    with ExitStack() as ctx:
        def sb(name, shape, dt=F32):
            return ctx.enter_context(nc.sbuf_tensor(name, shape, dt))

        def sem(name):
            return ctx.enter_context(nc.semaphore(name))

        adj = sb("adj", [P, BT, BLOCK])
        hi = sb("hi", [P, BT, BLOCK], F32R)
        lo = sb("lo", [P, BT, BLOCK], F32R)
        h = sb("h", [P, TILES, 2 * D])
        x = sb("x", [P, TILES, D])
        partial = sb("partial", [P, N])
        stat_two = sb("stat_two", [P, ST, 2, P], F32R)
        stat_one = sb("stat_one", [P, ST, 2, P], F32R)
        stat_raw = sb("stat_raw", [P, ST, P])
        tall = sb("tall", [P, BLOCK])
        lhs = sb("lhs", [P, BLOCK])
        w2 = sb("w2", [P, 2 * D])
        wl = sb("wl", [D + 1, 3, D])
        eye = sb("eye", [P, P])
        ones = sb("ones", [P, P], F32R)
        ones_raw = sb("ones_raw", [P, P])
        sum_pool = sb("sum_pool", [P, BLOCK])
        sum_dve = lhs
        zeros = sb("zeros", [P, P], F32R)
        xc = sb("xc", [P, BT, D])
        xsq = sb("xsq", [P, BT, D])
        degree_inv = sb("degree_inv", [P, TILES])
        rsum, mneg, vsum, var, std, r0, nt, rstd = [
            sb(name, [P, BT]) for name in ("rsum", "mneg", "vsum", "var", "std", "r0", "nt", "rstd")]

        ps = ctx.enter_context(nc.psum_tensor("ps", [P, 8 * CHUNK], F32))
        acc = [ps[:, 0:BLOCK], ps[:, BLOCK:2 * BLOCK]]
        one_acc, two_acc = acc
        degree = ps[:, 2 * BLOCK:3 * BLOCK]
        lin_two = ps[:, 2 * BLOCK:3 * BLOCK]
        lin = ps[:, 2 * BLOCK:2 * BLOCK + CHUNK]
        turned = ps[:, 3 * BLOCK:4 * BLOCK]

        adj_loaded = [sem(f"adj_loaded{k}") for k in range(BT)]
        x_loaded = sem("x_loaded")
        weights_loaded = sem("weights_loaded")
        used = sem("used")
        copied = sem("copied")
        split = sem("split")
        pass3_done = sem("pass3_done")
        twice_hi = sem("twice_hi")
        twice_split = sem("twice_split")
        squared = sem("squared")
        square_hi = sem("square_hi")
        square_split = sem("square_split")
        staged = sem("staged")
        stage_step = sem("stage_step")
        acc_taken_act = sem("acc_taken_act")
        acc_taken_dve = sem("acc_taken_dve")
        tall_half = sem("tall_half")
        h_copied = sem("h_copied")
        h_turned = sem("h_turned")
        tall_turned = sem("tall_turned")
        lhs_ready = sem("lhs_ready")
        lin_done = sem("lin_done")
        h_ready = sem("h_ready")
        added_pool = sem("added_pool")
        added_dve = sem("added_dve")
        degree_done = sem("degree_done")
        var_ready = sem("var_ready")
        std_ready = sem("std_ready")
        step = sem("step")
        out_ready = sem("out_ready")
        stored = sem("stored")

        def row_done(s, r):
            return BT * bodies_before(s, r + 1) + BT

        def cols(rb):
            return bass.ds(rb * BLOCK, BLOCK)

        def before(s, r):
            if static(r) and r == 0:
                return (s - 1, BLOCKS - 1, 1)
            return (s, r - 1, None)

        block = ctx.enter_context(nc.Block())

        @block.sync
        def _(sp):
            def load(o):
                if o.first:
                    if not o.corner:
                        sp.wait_ge(x_loaded, 32 * o.j)
                    tiles = bass.ds(o.j * BT, BT)
                    sp.dma_start(x[:, tiles, :], x_d[:, tiles, :]).then_inc(x_loaded, 16)
                    sp.dma_start(partial[:, bass.ds(o.j * BT * D, BT * D)].rearrange("p (t d) -> p t d", d=D),
                                 u_d[:, tiles, :]).then_inc(x_loaded, 16)
                for k in range(BT):
                    tile = in_register(sp, o.rb * TILES + o.jb * BT + k, BLOCKS * TILES - 1)
                    free = BT * o.loaded + k + 1
                    if o.s <= 2:
                        before = o.summed if o.s == 1 else paired_before(BLOCKS)
                        slots, added = (SUMS_POOL, added_pool) if k in SUMS_POOL else (SUMS_DVE, added_dve)
                        sums = in_register(sp, len(slots) * before + slots.index(k) + 1) if k in slots else None
                        if k in DIRECT_FIRST and o.s == 1 and (o.first or o.corner):
                            sp.wait_ge(used, free)
                        else:
                            sp.wait_ge(split, free)
                        if k in slots and (o.s == 1 or static(o.j) and o.j == 0 and o.corner):
                            sp.wait_ge(added, sums)
                    elif o.s == 3 or o.s == 4 and static(o.j) and o.j == 0 and o.corner or k in DIRECT:
                        sp.wait_ge(used, free)
                    else:
                        sp.wait_ge(square_split, len(SPLIT) * o.split + SPLIT.index(k) + 1)
                    sp.dma_start(adj[:, k, :], adj_d[tile]).then_inc(adj_loaded[k], 16)

            for s in range(1, PASSES + 1):
                row_blocks(sp, lambda r, parity, s=s: bodies(sp, s, r, load))

        @block.gpsimd
        def _(pool):
            def stage(o):
                s, own = o.s, half(o.s)
                pool.sem_clear(stage_step)
                if s == 1 and not o.paired:
                    if static(o.rb) and o.rb == 0:
                        pool.wait_ge(h_ready, o.j + 1)
                elif o.corner and static(o.j) and o.j == 0:
                    pool.wait_ge(h_ready, BLOCKS * s)
                elif o.paired:
                    pool.wait_ge(h_ready, BLOCKS * s + o.j + 1)
                steps = 0
                for k in range(BT):
                    pool.wait_ge(used, BT * o.loaded + BT - ST + k + 1)
                    tile = h[:, bass.ds(o.jb * BT + k, 1), :].rearrange("p a c -> p (a c)")
                    if o.first and k in DIRECT_FIRST:
                        nc.gpsimd.tensor_copy(stat_raw[:, k % ST, own], tile[:, own]).then_inc(staged, 1)
                        continue
                    if s >= 4 and k in DIRECT:
                        nc.gpsimd.tensor_copy(stat_raw[:, k % ST, :] if o.paired else stat_raw[:, k % ST, own],
                                              tile if o.paired else tile[:, own]).then_inc(staged, 1)
                        continue
                    if s == 3:
                        src, a, b = tile[:, own], stat_two[:, k % ST, 0, 0:D], stat_two[:, k % ST, 0, D:2 * D]
                    elif o.paired:
                        src, a, b = tile, stat_two[:, k % ST, 0, :], stat_two[:, k % ST, 1, :]
                    else:
                        src, a, b = tile[:, own], stat_one[:, k % ST, 0, own], stat_one[:, k % ST, 1, own]
                    nc.gpsimd.tensor_copy(a, src).then_inc(stage_step, 1)
                    steps += 1
                    if s == 3 and o.paired and k in SPLIT_TWICE:
                        a4, b4 = stat_two[:, k % ST, 1, half(4)], stat_two[:, k % ST, 1, half(3)]
                        nc.gpsimd.tensor_copy(a4, tile[:, half(4)]).then_inc(stage_step, 1)
                        steps += 1
                        pool.wait_ge(stage_step, steps)
                        nc.gpsimd.tensor_tensor(b4, tile[:, half(4)], a4.bitcast(F32), ALU.subtract).then_inc(stage_step, 1)
                        steps += 1
                    elif s == 3 and o.paired:
                        nc.gpsimd.tensor_copy(stat_raw[:, k % ST, half(4)], tile[:, half(4)]).then_inc(stage_step, 1)
                        steps += 1
                    pool.wait_ge(stage_step, steps)
                    nc.gpsimd.tensor_tensor(b, src, a.bitcast(F32), ALU.subtract).then_inc(staged, 1)
                    if s == 1 and o.paired and k in SUMS_POOL:
                        pool.wait_ge(adj_loaded[k], 16 * o.loaded + 16)
                        pool.wait_ge(acc_taken_dve, o.rb)
                        pool.wait_ge(added_pool, len(SUMS_POOL) * (o.summed + 1) + SUMS_POOL.index(k))
                        nc.gpsimd.tensor_tensor(sum_pool[:, :], sum_pool[:, :], adj[:, k, :],
                                                ALU.add).then_inc(added_pool, 1)

            def fill(half_tiles, value):
                nc.gpsimd.memset(half_tiles.bitcast(F32), value).then_inc(stage_step, 1)

            for s in range(1, PASSES + 1):
                if s in (1, 2, 5, 6):
                    pool.sem_clear(stage_step)
                    other = half(s + 1)
                    if s > 1:
                        pool.wait_ge(used, row_done(s - 1, BLOCKS - 1))
                    fill(stat_one[:, :, 0, other], 1.0 if s == 1 else 0.0)
                    fill(stat_one[:, :, 1, other], 0.0)
                    if s == 1:
                        nc.gpsimd.memset(stat_raw[:, :, other], 1.0).then_inc(stage_step, 1)
                    pool.wait_ge(stage_step, 3 if s == 1 else 2)
                if s == 3:
                    pool.sem_clear(stage_step)
                    pool.wait_ge(used, row_done(2, BLOCKS - 1))
                    nc.gpsimd.memset(stat_raw[:, :, half(3)], 0.0).then_inc(stage_step, 1)
                    pool.wait_ge(stage_step, 1)
                row_blocks(pool, lambda r, parity, s=s: bodies(pool, s, r, stage))
            for r in range(BLOCKS):
                rb = place(pool, PASSES, r)
                pool.wait_ge(out_ready, r + 1)
                pool.dma_start(out_d[:, rb * BT:rb * BT + BT, :], x[:, rb * BT:rb * BT + BT, :]).then_inc(stored, 16)
            pool.wait_ge(stored, 16 * BLOCKS)

        @block.tensor
        def _(pe):
            def products(out, st, k, moving, start=False):
                for m in moving:
                    for c in range(0, BLOCK, CHUNK):
                        last = nc.tensor.matmul(out[:, c:c + CHUNK], st, m[:, k, c:c + CHUNK], start=start, stop=False,
                                                skip_group_check=True)
                    start = False
                return last

            def clear(out, whole):
                for c in range(0, BLOCK, P if whole else CHUNK):
                    nc.tensor.matmul(out[:, c:c + P], zeros[:, :], zeros[:, :], start=c % CHUNK == 0, stop=False,
                                     skip_group_check=True)

            def multiply_square(o, k):
                if k in SPLIT_TWICE:
                    pe.wait_ge(twice_split, len(SPLIT_TWICE) * o.squared + SPLIT_TWICE.index(k) + 1)
                    last = products(two_acc, stat_two[:, k % ST, 1, :], k, (hi, lo))
                else:
                    pe.wait_ge(squared, BT * o.squared + k + 1)
                    last = products(two_acc, stat_raw[:, k % ST, :], k, (adj,))
                last.then_inc(used, 1)

            def multiply(o, parity, steps):
                s, own = o.s, half(o.s)
                for k in range(BT):
                    pe.wait_ge(staged, BT * o.loaded + k + 1)
                    start = o.corner and k == 0
                    if o.first and k in DIRECT_FIRST:
                        pe.wait_ge(adj_loaded[k], 16 * o.loaded + 16)
                    elif s <= 3:
                        pe.wait_ge(split, BT * o.loaded + BT + k + 1)
                    elif k in DIRECT:
                        pe.wait_ge(squared, BT * o.squared + k + 1)
                    else:
                        pe.wait_ge(square_split, len(SPLIT) * o.split + len(SPLIT) + SPLIT.index(k) + 1)
                    if s == 3:
                        last = products(one_acc, stat_two[:, k % ST, 0, :], k, (hi, lo), start)
                        if o.paired:
                            if k in SPLIT_TWICE:
                                last.then_inc(pass3_done, 1)
                            if k >= SQUARE_LAG:
                                multiply_square(o, k - SQUARE_LAG)
                            continue
                    elif o.first and k in DIRECT_FIRST:
                        last = products(one_acc, stat_raw[:, k % ST, :], k, (adj,))
                    elif s >= 4 and k in DIRECT:
                        if o.paired:
                            last = products(acc[parity], stat_raw[:, k % ST, :], k, (adj,))
                        else:
                            last = products(acc[parity][own, :], stat_raw[:, k % ST, own], k, (adj,))
                    else:
                        out = acc[parity] if s > 1 else two_acc if o.paired else one_acc
                        st = stat_two if o.paired else stat_one
                        products(out, st[:, k % ST, 0, :], k, (hi, lo), start)
                        last = products(out, st[:, k % ST, 1, :], k, (hi,))
                        if s == 1 and o.paired and k not in SUMS_POOL + SUMS_DVE:
                            last = products(degree, ones[:, :], k, (hi, lo))
                    last.then_inc(used, 1)
                    for do in steps.get(k, ()):
                        do()
                if s == 3 and o.paired:
                    for k in range(BT - SQUARE_LAG, BT):
                        multiply_square(o, k)

            def turn_h(r):
                pe.wait_ge(h_copied, r + 1)
                pe.wait_ge(tall_half, BLOCKS + r)
                for t in range(BT):
                    last = nc.tensor.transpose(turned[:, t * P:(t + 1) * P], lhs[:, t * P:(t + 1) * P], eye[:, :])
                last.then_inc(h_turned, 1)

            def turn_sums(s, r):
                pe.wait_ge(acc_taken_dve, (s - 1) * BLOCKS + r + 1)
                pe.wait_ge(tall_half, (s - 1) * BLOCKS + r + 1)
                for t in range(BT):
                    last = nc.tensor.transpose(turned[:, t * P:(t + 1) * P], tall[:, t * P:(t + 1) * P], eye[:, :])
                last.then_inc(tall_turned, 1)

            def linear(s, r):
                w, to, n = (w2[:, :], lin_two, 2 * D) if s == 2 else (wl[:, LINEAR[s] - 1, :], lin, D)
                src = tall[:, :] if s == 2 else lhs[0:D + 1, :]
                if s > 2:
                    pe.wait_ge(acc_taken_dve, BLOCKS * (s - 1) + r + 1)
                else:
                    pe.wait_ge(lhs_ready, r + 1)
                    pe.wait_ge(tall_half, BLOCKS + r + 1)
                for t in range(BT):
                    last = nc.tensor.matmul(to[:, t * n:(t + 1) * n], src[:, t * P:(t + 1) * P], w, start=True, stop=True)
                last.then_inc(lin_done, 1)

            def steps_behind(s, r):
                if s in (1, 3):
                    return {PE_AT: [lambda: turn_sums(s, r)]}
                if s == 2:
                    return {TURN_H_AT: [lambda: turn_h(r)], PE_AT: [lambda: linear(s, r)]}
                return {PE_AT: [lambda: linear(s, r)]}

            pe.wait_ge(used, BT)
            pe.wait_ge(split, BT)
            pe.wait_ge(weights_loaded, 48)
            for s in range(1, PASSES + 1):
                def row(r, parity, s=s):
                    first = static(r) and r == 0
                    rows = BLOCKS * (s - 1) + r
                    if s > 1 or not first:
                        ago = 0 if s in (1, 3) or first else 1
                        pe.wait_ge(acc_taken_dve, rows - ago)
                        if s not in (2, 3, PASSES) or first and s != 3:
                            pe.wait_ge(acc_taken_act, rows - ago - (BLOCKS if s > 2 else 0))
                        elif s == 3 and not first:
                            pe.wait_ge(acc_taken_act, BLOCKS + r)
                    if s in (1, 3):
                        clear(two_acc, first)
                    if s == 1:
                        clear(degree, first)
                    behind = {} if first else steps_behind(*before(s, r)[:2])
                    bodies(pe, s, r, lambda o: multiply(o, parity, behind if o.corner else {}))
                    if s == 1 and not first:
                        pe.wait_ge(added_pool, len(SUMS_POOL) * (paired_before(r + 1) + 1))
                        pe.wait_ge(added_dve, len(SUMS_DVE) * (paired_before(r + 1) + 1))
                        products(degree, ones_raw[:, :], 0, (sum_pool[:, :].unsqueeze(1),
                                                             sum_dve[:, :].unsqueeze(1))).then_inc(degree_done, 1)
                row_blocks(pe, row)
                for do in [do for _, dos in sorted(steps_behind(s, BLOCKS - 1).items()) for do in dos]:
                    do()

        @block.scalar
        def _(act):
            act.dma_start(w2[:, :], w2_d).then_inc(weights_loaded, 16)
            act.dma_start(wl[:, :, :], wl_d).then_inc(weights_loaded, 16)
            act.dma_start(eye[:, :], eye_d).then_inc(weights_loaded, 16)

            def root(n):
                act.wait_ge(var_ready, n + 1)
                nc.scalar.activation(std[:, :], var[:, :], ACT.Sqrt).then_inc(std_ready, 1)

            def square(o, k):
                nc.scalar.activation(adj[:, k, :], adj[:, k, :], ACT.Square).then_inc(squared, 1)

            def square_behind(o, k):
                act.wait_ge(split, BT * o.loaded + BT + k + 1)
                square(o, k)

            def prepare(o, steps):
                s = o.s
                if s == 1 and static(o.rb) and o.rb == 0:
                    root(o.j)
                for k in range(BT):
                    act.wait_ge(adj_loaded[k], 16 * o.loaded + 16)
                    if o.first and k in DIRECT_FIRST:
                        continue
                    if s <= 3:
                        act.wait_ge(used, BT * o.loaded + k + 1)
                        nc.scalar.activation(hi[:, k, :], adj[:, k, :], ACT.Copy).then_inc(copied, o.counts(k))
                        if s == 3 and o.paired and k >= 1:
                            square_behind(o, k - 1)
                    else:
                        square(o, k)
                    for do in steps.get(k, ()):
                        do()
                if s == 3 and o.paired:
                    square_behind(o, BT - 1)

            def take(s, r, parity):
                rb = place(act, s, r)
                done = in_register(act, row_done(s, r))
                to = partial[half(s + 1), cols(rb)]
                n = (BLOCKS if s == 2 else 2 * BLOCKS) + r
                if s == 2:
                    act.wait_ge(h_turned, r + 1)
                    nc.scalar.activation(tall[D:2 * D, :], turned[D:2 * D, :], ACT.Copy).then_inc(tall_half, 1)
                    return
                act.wait_ge(used, done)
                if s == 1:
                    nc.scalar.activation(tall[:, :], one_acc, ACT.Copy).then_inc(tall_half, 1)
                    nc.scalar.activation(to, two_acc[half(2), :], ACT.Copy).then_inc(acc_taken_act, 1)
                elif s == 3:
                    nc.scalar.activation(tall[D:2 * D, :], one_acc[D:2 * D, :], ACT.Copy).then_inc(tall_half, 1)
                    nc.scalar.activation(to, two_acc[half(4), :], ACT.Copy)
                    nc.scalar.activation(lhs[half(4), :], two_acc[half(3), :], ACT.Copy).then_inc(acc_taken_act, 1)
                elif s < PASSES:
                    nc.scalar.activation(to, acc[parity][half(s + 1), :], ACT.Copy).then_inc(acc_taken_act, 1)

            def copy_h(r):
                rb = place(act, 2, r)
                act.wait_ge(h_ready, 2 * BLOCKS)
                act.wait_ge(tall_half, BLOCKS + r)
                nc.scalar.activation(lhs[:, :].rearrange("p (t c) -> p t c", t=BT), h[:, bass.ds(rb * BT, BT), :],
                                     ACT.Copy).then_inc(h_copied, 1)

            def steps_behind(s, r, parity):
                steps = {}
                if s == 2:
                    steps[TURN_H_AT] = [lambda: copy_h(r)]
                steps.setdefault(STEPS_AT[s][0], []).append(lambda: take(s, r, parity))
                if s in NORM:
                    steps.setdefault(STEPS_AT[s][2], []).append(lambda: root(BLOCKS * (1 + NORM[s]) + r))
                return steps

            for s in range(1, PASSES + 1):
                def row(r, parity, s=s):
                    behind = {}
                    if s > 1 or not (static(r) and r == 0):
                        behind = steps_behind(*before(s, r)[:2], 1 - parity)
                    bodies(act, s, r, lambda o: prepare(o, behind if o.corner else {}))
                row_blocks(act, row)

        @block.vector
        def _(dve):
            count = [0]

            def begin():
                dve.sem_clear(step)
                count[0] = 0

            def link(ins):
                count[0] += 1
                ins.then_inc(step, 1)
                dve.wait_ge(step, count[0])

            def wide(v):
                return v[:, :].unsqueeze(2).broadcast_to([P, BT, D])

            def norm_begin(xb):
                link(nc.vector.tensor_reduce(rsum[:, :], xb, AX, ALU.add))
                link(nc.vector.tensor_scalar(mneg[:, :], rsum[:, :], -1.0 / D, None, ALU.mult))
                link(nc.vector.tensor_tensor(xc[:, :, :], xb, wide(mneg), ALU.add))
                link(nc.vector.tensor_tensor(xsq[:, :, :], xc[:, :, :], xc[:, :, :], ALU.mult))
                link(nc.vector.tensor_reduce(vsum[:, :], xsq[:, :, :], AX, ALU.add))
                nc.vector.tensor_scalar(var[:, :], vsum[:, :], 1.0 / D, EPS, ALU.mult, ALU.add).then_inc(var_ready, 1)

            def norm_end(n, hb, keep=None):
                dve.wait_ge(std_ready, n + 1)
                link(nc.vector.reciprocal(r0[:, :], std[:, :]))
                link(nc.vector.tensor_tensor(nt[:, :], r0[:, :], r0[:, :], ALU.mult))
                link(nc.vector.tensor_tensor(nt[:, :], nt[:, :], var[:, :], ALU.mult))
                link(nc.vector.tensor_scalar(nt[:, :], nt[:, :], -0.5, 1.5, ALU.mult, ALU.add))
                link(nc.vector.tensor_tensor(rstd[:, :], r0[:, :], nt[:, :], ALU.mult))
                if keep is None:
                    nc.vector.scalar_tensor_tensor(hb, xc[:, :, :], 0.0, wide(rstd), ALU.max,
                                                   ALU.mult).then_inc(h_ready, 1)
                    return
                link(nc.vector.scalar_tensor_tensor(xsq[:, :, :], xc[:, :, :], 0.0, wide(rstd), ALU.max, ALU.mult))
                link(nc.vector.tensor_scalar(xc[:, :, :], keep, KEEP_FROM, KEEP_SCALE, ALU.is_ge, ALU.mult))
                nc.vector.tensor_tensor(hb, xsq[:, :, :], xc[:, :, :], ALU.mult).then_inc(h_ready, 1)

            nc.vector.memset(zeros[:, :].bitcast(F32), 0.0).then_inc(used, BT)
            nc.vector.memset(ones[:, :].bitcast(F32), 1.0).then_inc(split, BT)
            nc.vector.memset(ones_raw[:, :], 1.0).then_inc(square_split, len(SPLIT))
            dve.wait_ge(square_split, len(SPLIT))
            dve.sem_inc(added_pool, len(SUMS_POOL))
            dve.sem_inc(added_dve, len(SUMS_DVE))
            dve.sem_inc(degree_done, 1)

            def split_square(o, k):
                n = len(SPLIT_TWICE) * o.squared + SPLIT_TWICE.index(k) + 1
                dve.wait_ge(squared, BT * o.squared + k + 1)
                dve.wait_ge(pass3_done, n)
                nc.vector.tensor_scalar(hi[:, k, :], adj[:, k, :], 1.0, None, ALU.mult).then_inc(twice_hi, 1)
                dve.wait_ge(twice_hi, n)
                nc.vector.tensor_tensor(lo[:, k, :], adj[:, k, :], hi[:, k, :].bitcast(F32),
                                        ALU.subtract).then_inc(twice_split, 1)

            def prepare(o, steps):
                s = o.s
                if s == 1 and static(o.rb) and o.rb == 0:
                    begin()
                    dve.wait_ge(x_loaded, 32 * o.j + 32)
                    norm_begin(x[:, bass.ds(o.j * BT, BT), :])
                    norm_end(o.j, h[:, bass.ds(o.j * BT, BT), half(1)],
                             keep=partial[:, bass.ds(o.j * BT * D, BT * D)].rearrange("p (t d) -> p t d", d=D))
                for k in range(BT):
                    if o.first and k in DIRECT_FIRST:
                        continue
                    if s <= 3:
                        dve.wait_ge(copied, BT * o.loaded + k + 1)
                        nc.vector.tensor_tensor(lo[:, k, :], adj[:, k, :], hi[:, k, :].bitcast(F32),
                                                ALU.subtract).then_inc(split, o.counts(k))
                        if s == 1 and o.paired and k in SUMS_DVE:
                            dve.wait_ge(added_dve, len(SUMS_DVE) * (o.summed + 1) + SUMS_DVE.index(k))
                            nc.vector.tensor_tensor(sum_dve[:, :], sum_dve[:, :], adj[:, k, :],
                                                    ALU.add).then_inc(added_dve, 1)
                        if s == 3 and o.paired and k - TWICE_LAG in SPLIT_TWICE:
                            split_square(o, k - TWICE_LAG)
                    elif k in SPLIT:
                        n = len(SPLIT) * o.split + SPLIT.index(k) + 1
                        dve.wait_ge(squared, BT * o.squared + k + 1)
                        dve.wait_ge(used, BT * o.loaded + k + 1)
                        nc.vector.tensor_scalar(hi[:, k, :], adj[:, k, :], 1.0, None, ALU.mult).then_inc(square_hi, 1)
                        dve.wait_ge(square_hi, n)
                        nc.vector.tensor_tensor(lo[:, k, :], adj[:, k, :], hi[:, k, :].bitcast(F32),
                                                ALU.subtract).then_inc(square_split, 1)
                    for do in steps.get(k, ()):
                        do()

            def steps_behind(s, r, parity):
                def names():
                    rb = place(dve, s, r)
                    tiles = bass.ds(rb * BT, BT)
                    return rb, x[:, tiles, :], h[:, tiles, half(s)], h[:, tiles, half(s + 1)]

                def take():
                    rb = place(dve, s, r)
                    own = partial[half(s), cols(rb)]
                    begin()
                    dve.wait_ge(used, row_done(s, r))
                    if s == 1:
                        dve.wait_ge(tall_half, r + 1)
                        dve.wait_ge(degree_done, r + 1)
                        nc.vector.memset(sum_pool[:, :], 0.0)
                        nc.vector.memset(sum_dve[:, :], 0.0)
                        link(nc.vector.tensor_tensor(tall[0:D, :], tall[0:D, :], two_acc[0:D, :], ALU.add))
                        nc.vector.tensor_tensor(tall[D:2 * D, :], tall[D:2 * D, :], degree[D:2 * D, :],
                                                ALU.add).then_inc(acc_taken_dve, 1)
                    elif s == 2:
                        nc.vector.tensor_tensor(tall[0:D, :], acc[parity][half(2), :], own,
                                                ALU.add).then_inc(lhs_ready, 1)
                        nc.vector.tensor_scalar(partial[half(3), cols(rb)], acc[parity][half(3), :], 1.0, None,
                                                ALU.mult).then_inc(acc_taken_dve, 1)
                    elif s == 3:
                        nc.vector.tensor_tensor(tall[0:D, :], one_acc[0:D, :], own, ALU.add).then_inc(acc_taken_dve, 1)
                        dve.wait_ge(acc_taken_act, BLOCKS + r + 1)
                        two = partial[half(4), cols(rb)]
                        link(nc.vector.tensor_tensor(two, two, lhs[half(4), :], ALU.add))
                        if static(r):
                            link(nc.vector.memset(lhs[D:D + 1, :], 1.0))
                    else:
                        nc.vector.tensor_tensor(lhs[0:D, :], acc[parity][half(s), :], own,
                                                ALU.add).then_inc(acc_taken_dve, 1)

                def middle():
                    rb, xb, own, nxt = names()
                    tiles = bass.ds(rb * BT, BT)
                    sums = turned.rearrange("p (t c) -> p t c", t=BT)
                    lint = lin.rearrange("p (t c) -> p t c", t=BT)
                    if s == 1:
                        dve.wait_ge(tall_turned, r + 1)
                        link(nc.vector.tensor_tensor(xb, sums[:, :, 0:D], xb, ALU.add))
                        link(nc.vector.tensor_scalar(degree_inv[:, tiles].unsqueeze(2), sums[:, :, D:D + 1], 1.0, None,
                                                     ALU.max))
                        link(nc.vector.reciprocal(degree_inv[:, tiles], degree_inv[:, tiles]))
                        norm_begin(xb)
                    elif s == 2:
                        dve.wait_ge(lin_done, r + 1)
                        two = lin_two.rearrange("p (t c) -> p t c", t=BT)
                        link(nc.vector.tensor_tensor(xc[:, :, :], two[:, :, 0:D],
                                                     degree_inv[:, tiles].unsqueeze(2).broadcast_to([P, BT, D]), ALU.mult))
                        link(nc.vector.tensor_tensor(xc[:, :, :], two[:, :, D:2 * D], xc[:, :, :], ALU.add))
                        link(nc.vector.scalar_tensor_tensor(xb, xc[:, :, :], 0.0, xb, ALU.max, ALU.add))
                        norm_begin(xb)
                    elif s == 3:
                        dve.wait_ge(tall_turned, BLOCKS + r + 1)
                        link(nc.vector.tensor_reduce(xc[:, :, :], turned.rearrange("p (t a c) -> p t c a", t=BT, a=2),
                                                     AX, ALU.add))
                        link(nc.vector.tensor_tensor(xsq[:, :, :], xc[:, :, :], own, ALU.mult))
                        link(nc.vector.tensor_reduce(rsum[:, :], xsq[:, :, :], AX, ALU.add))
                        link(nc.vector.tensor_scalar(mneg[:, :], rsum[:, :], -0.01, 1.0, ALU.mult, ALU.add))
                        link(nc.vector.scalar_tensor_tensor(xb, own, -0.1, xb, ALU.mult, ALU.add))
                        link(nc.vector.tensor_tensor(xb, xb, wide(mneg), ALU.add))
                        norm_begin(xb)
                    elif s < PASSES:
                        dve.wait_ge(lin_done, LINEAR[s] * BLOCKS + r + 1)
                        nc.vector.tensor_scalar(nxt, lint, 1.0, None, ALU.mult).then_inc(h_ready, 1)
                    else:
                        dve.wait_ge(lin_done, LINEAR[s] * BLOCKS + r + 1)
                        nc.vector.tensor_tensor(xb, lint, xb, ALU.add).then_inc(out_ready, 1)

                def end():
                    rb, xb, own, nxt = names()
                    norm_end(BLOCKS * (1 + NORM[s]) + r, nxt)

                steps = {}
                for at, do in zip(STEPS_AT[s], (take, middle, end) if s in NORM else (take, middle)):
                    steps.setdefault(at, []).append(do)
                return steps

            for s in range(1, PASSES + 1):
                def row(r, parity, s=s):
                    behind = {}
                    if s > 1 or not (static(r) and r == 0):
                        behind = steps_behind(*before(s, r)[:2], 1 - parity)
                    bodies(dve, s, r, lambda o: prepare(o, behind if o.corner else {}))
                row_blocks(dve, row)
            for _, dos in sorted(steps_behind(PASSES, BLOCKS - 1, 1).items()):
                for do in dos:
                    do()


def kernel(x, adj, L0_gnn_u, L1_gnn_W, L2_gnn_t, L3_gnn_W0, L3_gnn_b0, L3_gnn_W1, L3_gnn_b1, L3_gnn_W2, L3_gnn_b2):
    import numpy as np
    import concourse.bacc as bacc
    from concourse.bass_utils import run_bass_kernel_spmd

    def rows_on_partitions(a):
        return np.ascontiguousarray(np.asarray(a).reshape(TILES, P, D).transpose(1, 0, 2))

    weights = [(L3_gnn_W0, L3_gnn_b0), (L3_gnn_W1, L3_gnn_b1), (L3_gnn_W2, L3_gnn_b2)]
    w2 = np.zeros((2 * D, 2 * D), np.float32)
    w2[0:D, 0:D] = np.asarray(L1_gnn_W)[:, D:].T
    w2[D:, D:] = np.asarray(L1_gnn_W)[:, 0:D].T
    arrays = {
        "x_in": rows_on_partitions(x),
        "adj_in": np.ascontiguousarray(np.asarray(adj).reshape(BLOCKS, BLOCK, TILES, P).transpose(0, 2, 3, 1)).reshape(
            BLOCKS * TILES, P, BLOCK),
        "u_in": rows_on_partitions(L0_gnn_u),
        "w2_in": w2,
        "wl_in": np.ascontiguousarray(np.stack([np.concatenate([np.asarray(w).T, np.asarray(b)[None, :]], axis=0)
                                                for w, b in weights], axis=1)),
        "eye_in": np.eye(P, dtype=np.float32),
    }
    nc = bacc.Bacc("TRN2", target_bir_lowering=False, num_devices=1)
    aps = [nc.dram_tensor(name, a.shape, mybir.dt.from_np(a.dtype), kind="ExternalInput").ap()
           for name, a in arrays.items()]
    out = nc.dram_tensor("out", (P, TILES, D), F32, kind="ExternalOutput").ap()
    build(nc, *aps, out)
    r = run_bass_kernel_spmd(nc, [arrays], core_ids=[0])
    return np.ascontiguousarray(r.results[0]["out"].transpose(1, 0, 2)).reshape(N, D)
```
